# Optimizing a Trainium2 kernel written in Bass

```python
import numpy as np
import jax
import jax.numpy as jnp

def _softmax(x, axis=-1):
    return jax.nn.softmax(x, axis=axis)

def _gelu(x):
    return jax.nn.gelu(x, approximate=True)

def _silu(x):
    return jax.nn.silu(x)

def _sigmoid(x):
    return jax.nn.sigmoid(x)

def _layernorm(x, axis=-1, eps=1e-05):
    m = jnp.mean(x, axis=axis, keepdims=True)
    v = jnp.var(x, axis=axis, keepdims=True)
    return (x - m) / jnp.sqrt(v + eps)

def _scatter_add(tgt, idx, src, axis=0):
    return tgt.at[idx].add(src)

def _segment_sum(src, seg, n):
    return jax.ops.segment_sum(src, seg, n)
kernel_name = 'mk_dlrm_tower_d1_rec_r8_fe4bda'

def setup_inputs(seed: int=0):
    np.random.seed(seed)
    _w = jnp.asarray

    def _rec_inputs():
        import jax
        import jax.numpy as jnp
        _tk = jax.random.key(seed)
        ids = jnp.stack([jax.random.randint(jax.random.fold_in(_tk, 200 + f), (2048,), 0, v, jnp.int32) for f, v in enumerate([12500, 12500, 1250, 125000, 1000, 1000, 1000, 1250, 1000, 1000, 1000, 1000, 1250, 12500, 1000, 1250, 1000, 1250, 1000, 1000, 12500, 1000, 12500, 1250, 12500, 1250])], axis=1)
        tbl_0 = 0.05 * jax.random.normal(jax.random.fold_in(_tk, 500 + 0), (12500, 128), jnp.float32)
        tbl_1 = 0.05 * jax.random.normal(jax.random.fold_in(_tk, 500 + 1), (12500, 128), jnp.float32)
        tbl_2 = 0.05 * jax.random.normal(jax.random.fold_in(_tk, 500 + 2), (1250, 128), jnp.float32)
        tbl_3 = 0.05 * jax.random.normal(jax.random.fold_in(_tk, 500 + 3), (125000, 128), jnp.float32)
        tbl_4 = 0.05 * jax.random.normal(jax.random.fold_in(_tk, 500 + 4), (1000, 128), jnp.float32)
        tbl_5 = 0.05 * jax.random.normal(jax.random.fold_in(_tk, 500 + 5), (1000, 128), jnp.float32)
        tbl_6 = 0.05 * jax.random.normal(jax.random.fold_in(_tk, 500 + 6), (1000, 128), jnp.float32)
        tbl_7 = 0.05 * jax.random.normal(jax.random.fold_in(_tk, 500 + 7), (1250, 128), jnp.float32)
        tbl_8 = 0.05 * jax.random.normal(jax.random.fold_in(_tk, 500 + 8), (1000, 128), jnp.float32)
        tbl_9 = 0.05 * jax.random.normal(jax.random.fold_in(_tk, 500 + 9), (1000, 128), jnp.float32)
        tbl_10 = 0.05 * jax.random.normal(jax.random.fold_in(_tk, 500 + 10), (1000, 128), jnp.float32)
        tbl_11 = 0.05 * jax.random.normal(jax.random.fold_in(_tk, 500 + 11), (1000, 128), jnp.float32)
        tbl_12 = 0.05 * jax.random.normal(jax.random.fold_in(_tk, 500 + 12), (1250, 128), jnp.float32)
        tbl_13 = 0.05 * jax.random.normal(jax.random.fold_in(_tk, 500 + 13), (12500, 128), jnp.float32)
        tbl_14 = 0.05 * jax.random.normal(jax.random.fold_in(_tk, 500 + 14), (1000, 128), jnp.float32)
        tbl_15 = 0.05 * jax.random.normal(jax.random.fold_in(_tk, 500 + 15), (1250, 128), jnp.float32)
        tbl_16 = 0.05 * jax.random.normal(jax.random.fold_in(_tk, 500 + 16), (1000, 128), jnp.float32)
        tbl_17 = 0.05 * jax.random.normal(jax.random.fold_in(_tk, 500 + 17), (1250, 128), jnp.float32)
        tbl_18 = 0.05 * jax.random.normal(jax.random.fold_in(_tk, 500 + 18), (1000, 128), jnp.float32)
        tbl_19 = 0.05 * jax.random.normal(jax.random.fold_in(_tk, 500 + 19), (1000, 128), jnp.float32)
        tbl_20 = 0.05 * jax.random.normal(jax.random.fold_in(_tk, 500 + 20), (12500, 128), jnp.float32)
        tbl_21 = 0.05 * jax.random.normal(jax.random.fold_in(_tk, 500 + 21), (1000, 128), jnp.float32)
        tbl_22 = 0.05 * jax.random.normal(jax.random.fold_in(_tk, 500 + 22), (12500, 128), jnp.float32)
        tbl_23 = 0.05 * jax.random.normal(jax.random.fold_in(_tk, 500 + 23), (1250, 128), jnp.float32)
        tbl_24 = 0.05 * jax.random.normal(jax.random.fold_in(_tk, 500 + 24), (12500, 128), jnp.float32)
        tbl_25 = 0.05 * jax.random.normal(jax.random.fold_in(_tk, 500 + 25), (1250, 128), jnp.float32)
        _rk = jax.random.fold_in(_tk, 7)
        r_dense_features = 7.22013e-05 + 1.00017 * jax.random.normal(jax.random.fold_in(_rk, 101), (2048, 128), jnp.float32)
        W_top1 = 0.0456912 * jax.random.normal(jax.random.fold_in(_tk, 801), (479, 512), jnp.float32)
        W_top2 = 0.0441942 * jax.random.normal(jax.random.fold_in(_tk, 802), (512, 256), jnp.float32)
        W_top3 = 0.0625 * jax.random.normal(jax.random.fold_in(_tk, 803), (256, 1), jnp.float32)
        b_top1 = jnp.zeros((512,), jnp.float32)
        b_top2 = jnp.zeros((256,), jnp.float32)
        return (r_dense_features, ids, tbl_0, tbl_1, tbl_2, tbl_3, tbl_4, tbl_5, tbl_6, tbl_7, tbl_8, tbl_9, tbl_10, tbl_11, tbl_12, tbl_13, tbl_14, tbl_15, tbl_16, tbl_17, tbl_18, tbl_19, tbl_20, tbl_21, tbl_22, tbl_23, tbl_24, tbl_25, W_top1, b_top1, W_top2, b_top2, W_top3)
    r_dense_features, ids, tbl_0, tbl_1, tbl_2, tbl_3, tbl_4, tbl_5, tbl_6, tbl_7, tbl_8, tbl_9, tbl_10, tbl_11, tbl_12, tbl_13, tbl_14, tbl_15, tbl_16, tbl_17, tbl_18, tbl_19, tbl_20, tbl_21, tbl_22, tbl_23, tbl_24, tbl_25, W_top1, b_top1, W_top2, b_top2, W_top3 = _rec_inputs()

    def _L0_rec_setup():
        import jax, jax.numpy as jnp
        import numpy as np
        FEATURE_NUM = 27
        key = jax.random.key(seed)
        k1, k2 = jax.random.split(key)
        B, N, D = (8192, FEATURE_NUM - 1, 128)
        dense_features = jax.random.normal(k1, (B, D), dtype=jnp.float32)
        sparse_features = jax.random.normal(k2, (B, N, D), dtype=jnp.float32)
        return {'dense_features': dense_features, 'sparse_features': sparse_features}
    _L0_rec_all = _L0_rec_setup()
    _L0_rec_in = {k: v for k, v in _L0_rec_all.items() if k in ()}
    del _L0_rec_all
    return {'r_dense_features': r_dense_features, 'ids': ids, 'tbl_0': tbl_0, 'tbl_1': tbl_1, 'tbl_2': tbl_2, 'tbl_3': tbl_3, 'tbl_4': tbl_4, 'tbl_5': tbl_5, 'tbl_6': tbl_6, 'tbl_7': tbl_7, 'tbl_8': tbl_8, 'tbl_9': tbl_9, 'tbl_10': tbl_10, 'tbl_11': tbl_11, 'tbl_12': tbl_12, 'tbl_13': tbl_13, 'tbl_14': tbl_14, 'tbl_15': tbl_15, 'tbl_16': tbl_16, 'tbl_17': tbl_17, 'tbl_18': tbl_18, 'tbl_19': tbl_19, 'tbl_20': tbl_20, 'tbl_21': tbl_21, 'tbl_22': tbl_22, 'tbl_23': tbl_23, 'tbl_24': tbl_24, 'tbl_25': tbl_25, 'W_top1': W_top1, 'b_top1': b_top1, 'W_top2': W_top2, 'b_top2': b_top2, 'W_top3': W_top3}

def reference(r_dense_features, ids, tbl_0, tbl_1, tbl_2, tbl_3, tbl_4, tbl_5, tbl_6, tbl_7, tbl_8, tbl_9, tbl_10, tbl_11, tbl_12, tbl_13, tbl_14, tbl_15, tbl_16, tbl_17, tbl_18, tbl_19, tbl_20, tbl_21, tbl_22, tbl_23, tbl_24, tbl_25, W_top1, b_top1, W_top2, b_top2, W_top3):
    import jax
    import jax.numpy as jnp

    def _L0_rec_ref(dense_features, sparse_features):
        import jax, jax.numpy as jnp
        import numpy as np
        FEATURE_NUM = 27
        combined = jnp.concatenate([dense_features[:, None, :], sparse_features], axis=1)
        interactions = jnp.einsum('bfd,bgd->bfg', combined, combined)
        iu, ju = jnp.triu_indices(FEATURE_NUM, k=1)
        return interactions[:, iu, ju]
    e = jnp.stack([tbl_0[ids[:, 0]], tbl_1[ids[:, 1]], tbl_2[ids[:, 2]], tbl_3[ids[:, 3]], tbl_4[ids[:, 4]], tbl_5[ids[:, 5]], tbl_6[ids[:, 6]], tbl_7[ids[:, 7]], tbl_8[ids[:, 8]], tbl_9[ids[:, 9]], tbl_10[ids[:, 10]], tbl_11[ids[:, 11]], tbl_12[ids[:, 12]], tbl_13[ids[:, 13]], tbl_14[ids[:, 14]], tbl_15[ids[:, 15]], tbl_16[ids[:, 16]], tbl_17[ids[:, 17]], tbl_18[ids[:, 18]], tbl_19[ids[:, 19]], tbl_20[ids[:, 20]], tbl_21[ids[:, 21]], tbl_22[ids[:, 22]], tbl_23[ids[:, 23]], tbl_24[ids[:, 24]], tbl_25[ids[:, 25]]], axis=1)
    z = _L0_rec_ref(r_dense_features, e)
    z = z.reshape(z.shape[0], -1)
    h = jnp.concatenate([z, r_dense_features], axis=1)
    h = jnp.maximum(h @ W_top1 + b_top1, 0.0)
    h = jnp.maximum(h @ W_top2 + b_top2, 0.0)
    y = h @ W_top3
    return y

_drawn_inputs = setup_inputs


def setup_inputs(seed=0):
    import zlib

    import numpy as np

    out = dict(_drawn_inputs(seed))
    spreads = {'b_top1': (0.0, 0.1), 'b_top2': (0.0, 0.1)}
    factors = {}
    for name, (base, spread) in spreads.items():
        noise = np.random.default_rng([zlib.crc32(name.encode()), seed]).standard_normal(out[name].shape)
        drawn = base * np.exp(spread * noise) if base else spread * noise
        out[name] = jnp.asarray(drawn.astype(out[name].dtype))
    for name, factor in factors.items():
        out[name] = (out[name] * factor).astype(out[name].dtype)
    return out
```

```python
from contextlib import ExitStack

import concourse.bass as bass
from concourse import mybir

F32 = mybir.dt.float32
U32 = mybir.dt.uint32
ACT = mybir.ActivationFunctionType
ALU = mybir.AluOpType

P = 128
NT = 26
NF = NT + 1
SLOT = 32
S = P // SLOT
TPC = 4
Q = P // S
GQ = 8
NG = Q // GQ
TG = 4
NTG = -(-NF // TG)
NK = (NF - 1) // 2
WRAP = NF + NK
KT = 3
FPK = NF // KT
KP = FPK * NK


def dlrm_tower(nc, dense, ids, tables, w1_pairs, w1_dense, b1, w2, b2, w3, z_dram, out):
    B, D = dense.shape
    TILES = B // P
    NC = TILES // TPC
    CW = TPC * P
    N1 = w1_dense.shape[1]
    N2 = w2.shape[1]
    M1 = N1 // P
    M2 = N2 // P
    MLP_GROUPS = M1 + M2 + 1
    assert D == P and CW == 512 and NF * NK == NF * (NF - 1) // 2

    with ExitStack() as ctx:
        def sb(name, shape, dt=F32):
            return ctx.enter_context(nc.sbuf_tensor(name, shape, dt))

        def psum(name, shape):
            return ctx.enter_context(nc.psum_tensor(name, shape, F32))

        def sem(name):
            return ctx.enter_context(nc.semaphore(name))

        ident = sb("ident", [P, P])
        ids_sb = sb("ids_sb", [P, TILES * NT], U32)
        idx = sb("idx", [P, TPC, NT], U32)
        dense_sb = sb("dense_sb", [P, TILES * D])
        x = sb("x", [P, TPC, NF, D])
        xt = sb("xt", [P, 2, P, SLOT])
        dense_t = sb("dense_t", [P, NC, S, TPC, Q])
        zs = sb("zs", [P, 2, NF, TPC, Q])
        zt = sb("zt", [P, KT, CW])
        w1p_sb = sb("w1p_sb", [P, KT, N1])
        w1d_sb = sb("w1d_sb", [P, N1])
        w2_sb = sb("w2_sb", [P, M1, N2])
        w3_sb = sb("w3_sb", [P, M2])
        b1_sb = sb("b1_sb", [P, M1])
        b2_sb = sb("b2_sb", [P, M2])
        h1 = sb("h1", [P, M1, CW])
        h2 = sb("h2", [P, M2, CW])
        y_sb = sb("y_sb", [1, B])

        ps_t = psum("ps_t", [P, 2, TG, P])
        ps_g = psum("ps_g", [P, 2, GQ, P])
        ps_m = psum("ps_m", [P, 2, CW])

        ids_loaded = sem("ids_loaded")
        dense_loaded = sem("dense_loaded")
        weights_loaded = sem("weights_loaded")
        ident_zeroed = sem("ident_zeroed")
        ident_ready = sem("ident_ready")
        pad_zeroed = sem("pad_zeroed")
        idx_ready = sem("idx_ready")
        dense_ready = sem("dense_ready")
        x_loaded = [sem(f"x_loaded{i}") for i in range(TPC)]
        x_free = sem("x_free")
        tp_ready = sem("tp_ready")
        tp_evicted = sem("tp_evicted")
        dense_t_ready = sem("dense_t_ready")
        gram_ready = sem("gram_ready")
        gram_evicted = sem("gram_evicted")
        zs_free = sem("zs_free")
        z_stored = sem("z_stored")
        zt_loaded = sem("zt_loaded")
        mlp_ready = sem("mlp_ready")
        mlp_evicted = sem("mlp_evicted")
        y_stored = sem("y_stored")

        GRAM0 = 2 * NG
        Z_DMAS = 2 * S
        WEIGHTS = 6

        block = ctx.enter_context(nc.Block())

        @block.sync
        def _(sp):
            sp.dma_start(ids_sb[:], ids.bitcast(U32).rearrange("(p t) f -> p (t f)", p=P)).then_inc(ids_loaded, 16)
            sp.dma_start(dense_sb[:], dense.rearrange("(p t) d -> p (t d)", p=P)).then_inc(dense_loaded, 16)
            sp.dma_start(w1p_sb[0:KP], w1_pairs.rearrange("(k p) n -> p k n", k=KT)).then_inc(weights_loaded, 16)
            sp.dma_start(w1d_sb[:], w1_dense).then_inc(weights_loaded, 16)
            sp.dma_start(w2_sb[:], w2.rearrange("(k p) n -> p k n", p=P)).then_inc(weights_loaded, 16)
            with nc.allow_non_contiguous_dma(reason="a few hundred words, once"):
                sp.dma_start(w3_sb[:], w3.rearrange("(k p) o -> p (k o)", p=P)).then_inc(weights_loaded, 16)
                sp.dma_start(b1_sb[:], b1.rearrange("(k p) -> p k", p=P)).then_inc(weights_loaded, 16)
                sp.dma_start(b2_sb[:], b2.rearrange("(k p) -> p k", p=P)).then_inc(weights_loaded, 16)
            sp.sem_inc(zs_free, 2)
            with sp.Fori(0, NC) as c:
                sp.wait_ge(gram_evicted, (c + 1) * (TPC * NG) + GRAM0)
                sp.nop(nofuse=True)
                half = c % 2
                for s in range(S):
                    src = zs[SLOT * s:SLOT * s + NF, bass.ds(half, 1)].rearrange("p o g t q -> p (o g) (t q)")
                    dst = z_dram[0:NF * WRAP, s].rearrange("(f g) q -> f g q", f=NF)
                    sp.dma_start(dst[:, 0:NF], src).then_inc(z_stored, 16)
                    sp.dma_start(dst[:, NF:WRAP], src[:, 0:NK]).then_inc(z_stored, 16)
                sp.wait_ge(z_stored, (c + 1) * (16 * Z_DMAS))
                sp.nop(nofuse=True)
                sp.sem_inc(zs_free, 1)
                sp.wait_ge(mlp_evicted, c * MLP_GROUPS + 2)
                sp.nop(nofuse=True)
                for k in range(KT):
                    first = FPK * k * (WRAP + 1) + 1
                    rows = z_dram[first:first + FPK * (WRAP + 1)].rearrange("(f g) s q -> f g (s q)", f=FPK)
                    sp.dma_start(zt[0:KP, k, :], rows[:, 0:NK]).then_inc(zt_loaded, 16)
                sp.wait_ge(zt_loaded, (c + 1) * (16 * KT))
                sp.nop(nofuse=True)
            sp.wait_ge(mlp_evicted, NC * MLP_GROUPS + 2)
            sp.dma_start(out.rearrange("(o b) -> o b", o=1), y_sb[:]).then_inc(y_stored, 16)
            sp.wait_ge(y_stored, 16)

        @block.gpsimd
        def _(pool):
            nc.gpsimd.memset(ident[:], 0.0).then_inc(ident_zeroed, 1)
            nc.gpsimd.memset(xt[:, :, :, NF:SLOT], 0.0).then_inc(pad_zeroed, 1)
            pool.wait_ge(ident_zeroed, 1)
            nc.gpsimd.affine_select(out=ident[:], in_=ident[:], compare_op=ALU.not_equal, fill=1.0, base=0,
                                    pattern=[[-1, P]], channel_multiplier=1).then_inc(ident_ready, 1)
            with pool.Fori(0, NC) as c:
                for tl in range(TPC):
                    pool.wait_ge(idx_ready, c * TPC + (tl + 1))
                    pool.nop(nofuse=True)
                    pool.wait_ge(x_free, c * TPC + (tl + 1))
                    pool.nop(nofuse=True)
                    for f in range(NT):
                        pool.indirect_dma_start(
                            x[:, tl, 1 + f, :], None, tables[f],
                            bass.IndirectOffsetOnAxis(ap=idx[:, tl, f:f + 1], axis=0)).then_inc(x_loaded[tl], 16)

        @block.tensor
        def _(pe):
            def transposes(c, tl):
                pe.wait_ge(x_loaded[tl], (c + 1) * (16 * NT))
                pe.wait_ge(dense_ready, c * TPC + (tl + 1))
                for j in range(NTG):
                    pe.wait_ge(tp_evicted, c * (TPC * NTG) + (tl * NTG + j + 1))
                    fs = range(TG * j, min(TG * (j + 1), NF))
                    for f in fs:
                        mm = nc.tensor.transpose(ps_t[:, (tl * NTG + j) % 2, f - fs[0], :], x[:, tl, f, :], ident[:])
                    mm.then_inc(tp_ready, 1)
                pe.wait_ge(tp_ready, c * (TPC * NTG) + (tl + 1) * NTG)
                pe.sem_inc(x_free, 1)

            def grams(c, tl):
                pe.wait_ge(tp_evicted, c * (TPC * NTG) + ((tl + 1) * NTG + 2))
                for g in range(NG):
                    pe.wait_ge(gram_evicted, c * (TPC * NG) + (tl * NG + g - 1 + GRAM0))
                    for q in range(GQ):
                        a = (g * GQ + q) * S
                        mm = nc.tensor.matmul(
                            ps_g[:, g % 2, q, 0:S * NF].rearrange("p (s f) -> p s f", s=S),
                            xt[:, tl % 2, a:a + S, :].rearrange("p s f -> p (s f)"),
                            xt[:, tl % 2, a:a + S, 0:NF], start=True, stop=True)
                    mm.then_inc(gram_ready, 1)

            def perceptron(c):
                pe.wait_ge(zt_loaded, (c + 1) * (16 * KT))
                pe.wait_ge(dense_t_ready, (c + 1) * TPC)
                for m in range(M1):
                    pe.wait_ge(mlp_evicted, c * MLP_GROUPS + (max(m - 1, 0) + 2))
                    cols = slice(m * P, (m + 1) * P)
                    nc.tensor.matmul(ps_m[:, m % 2, :], w1d_sb[:, cols],
                                     dense_t[:, bass.ds(c, 1)].rearrange("p o s t q -> p (o s t q)"),
                                     start=True, stop=False)
                    for k in range(KT):
                        mm = nc.tensor.matmul(ps_m[:, m % 2, :], w1p_sb[0:KP, k, cols], zt[0:KP, k, :],
                                              start=False, stop=(k == KT - 1))
                    mm.then_inc(mlp_ready, 1)
                pe.wait_ge(mlp_evicted, c * MLP_GROUPS + (M1 + 2))
                for m in range(M2):
                    for k in range(M1):
                        mm = nc.tensor.matmul(ps_m[:, m % 2, :], w2_sb[:, k, m * P:(m + 1) * P], h1[:, k, :],
                                              start=(k == 0), stop=(k == M1 - 1))
                    mm.then_inc(mlp_ready, 1)
                pe.wait_ge(mlp_evicted, c * MLP_GROUPS + (M1 + M2 + 2))
                for k in range(M2):
                    mm = nc.tensor.matmul(ps_m[0:1, 0, :], w3_sb[:, k:k + 1], h2[:, k, :],
                                          start=(k == 0), stop=(k == M2 - 1))
                mm.then_inc(mlp_ready, 1)

            pe.wait_ge(ident_ready, 1)
            pe.wait_ge(pad_zeroed, 1)
            pe.sem_inc(x_free, TPC)
            transposes(0, 0)
            transposes(0, 1)
            grams(0, 0)
            pe.wait_ge(weights_loaded, 16 * WEIGHTS)
            with pe.Fori(0, NC - 1) as i:
                transposes(i, 2)
                grams(i, 1)
                transposes(i, 3)
                grams(i, 2)
                transposes(i + 1, 0)
                grams(i, 3)
                transposes(i + 1, 1)
                grams(i + 1, 0)
                perceptron(i)
            transposes(NC - 1, 2)
            grams(NC - 1, 1)
            transposes(NC - 1, 3)
            grams(NC - 1, 2)
            grams(NC - 1, 3)
            perceptron(NC - 1)

        @block.scalar
        def _(act):
            def evict_transposes(c, tl):
                act.wait_ge(gram_evicted, c * (TPC * NG) + ((tl - 1) * NG + GRAM0))
                for j in range(NTG):
                    n = min(TG, NF - TG * j)
                    act.wait_ge(tp_ready, c * (TPC * NTG) + (tl * NTG + j + 1))
                    src = ps_t[:, (tl * NTG + j) % 2]
                    if j == 0:
                        nc.scalar.copy(dense_t[:, bass.ds(c, 1), :, tl, :].rearrange("p o s q -> p (o s) q"),
                                       src[:, 0, :].rearrange("p (q s) -> p s q", s=S)).then_inc(dense_t_ready, 1)
                    nc.scalar.copy(xt[:, tl % 2, :, TG * j:TG * j + n],
                                   src[:, 0:n, :].rearrange("p f b -> p b f")).then_inc(tp_evicted, 1)

            def evict_perceptron(c):
                base = c * MLP_GROUPS
                for m in range(M1):
                    act.wait_ge(mlp_ready, base + (m + 1))
                    nc.scalar.activation(h1[:, m, :], ps_m[:, m % 2, :], ACT.Relu,
                                         bias=b1_sb[:, m:m + 1]).then_inc(mlp_evicted, 1)
                for m in range(M2):
                    act.wait_ge(mlp_ready, base + (M1 + m + 1))
                    nc.scalar.activation(h2[:, m, :], ps_m[:, m % 2, :], ACT.Relu,
                                         bias=b2_sb[:, m:m + 1]).then_inc(mlp_evicted, 1)
                act.wait_ge(mlp_ready, base + MLP_GROUPS)
                nc.scalar.copy(y_sb[:, bass.ds(c * CW, CW)], ps_m[0:1, 0, :]).then_inc(mlp_evicted, 1)

            act.sem_inc(tp_evicted, 2)
            act.sem_inc(mlp_evicted, 2)
            act.wait_ge(weights_loaded, 16 * WEIGHTS)
            evict_transposes(0, 0)
            evict_transposes(0, 1)
            with act.Fori(0, NC - 1) as i:
                evict_transposes(i, 2)
                evict_transposes(i, 3)
                evict_transposes(i + 1, 0)
                evict_transposes(i + 1, 1)
                evict_perceptron(i)
            evict_transposes(NC - 1, 2)
            evict_transposes(NC - 1, 3)
            evict_perceptron(NC - 1)

        @block.vector
        def _(dve):
            def stage(c, tl):
                t = c * TPC + tl
                nc.vector.tensor_copy(idx[:, tl, :], ids_sb[:, bass.ds(t * NT, NT)]).then_inc(idx_ready, 1)
                nc.vector.tensor_copy(x[:, tl, 0, :], dense_sb[:, bass.ds(t * D, D)]).then_inc(dense_ready, 1)

            def evict_grams(c, tl):
                half = c % 2
                if tl == 0:
                    dve.wait_ge(zs_free, c + 1)
                for g in range(NG):
                    dve.wait_ge(gram_ready, c * (TPC * NG) + (tl * NG + g + 1))
                    for s in range(S):
                        rows = slice(SLOT * s, SLOT * s + NF)
                        last = nc.vector.tensor_copy(
                            zs[rows, bass.ds(half, 1), :, tl, g * GQ:(g + 1) * GQ].rearrange("p o g q -> p (o g) q"),
                            ps_g[rows, g % 2, :, s * NF:(s + 1) * NF].rearrange("p q g -> p g q"))
                    last.then_inc(gram_evicted, 1)

            dve.sem_inc(gram_evicted, GRAM0)
            dve.wait_ge(ids_loaded, 16)
            dve.wait_ge(dense_loaded, 16)
            for tl in range(3):
                stage(0, tl)
            evict_grams(0, 0)
            stage(0, 3)
            with dve.Fori(0, NC - 1) as i:
                for tl in range(1, TPC):
                    evict_grams(i, tl)
                    stage(i + 1, tl - 1)
                evict_grams(i + 1, 0)
                stage(i + 1, 3)
            for tl in range(1, TPC):
                evict_grams(NC - 1, tl)


_TABLES = [f"tbl_{f}" for f in range(NT)]


def kernel(**inputs):
    import numpy as _np
    import concourse.bacc as _bacc
    from concourse import mybir as _mybir
    from concourse.bass_utils import run_bass_kernel_spmd as _run

    nc = _bacc.Bacc("TRN2", target_bir_lowering=False, num_devices=1)
    pair = [[0] * NF for _ in range(NF)]
    n = 0
    for f in range(NF):
        for g in range(f + 1, NF):
            pair[f][g] = pair[g][f] = n
            n += 1
    order = _np.array([pair[f][(f + k) % NF] for f in range(NF) for k in range(1, NK + 1)])
    w1 = _np.asarray(inputs["W_top1"])
    given = {name: _np.asarray(inputs[name]) for name in
             ["r_dense_features", "ids"] + _TABLES + ["b_top1", "W_top2", "b_top2", "W_top3"]}
    given["w1_pairs"] = w1[order]
    given["w1_dense"] = w1[n:]
    arrays, args = {}, {}
    for name, a in given.items():
        a = _np.ascontiguousarray(a)
        arrays[f"in_{name}"] = a
        args[name] = nc.dram_tensor(f"in_{name}", a.shape, _mybir.dt.from_np(a.dtype), kind="ExternalInput").ap()
    B = given["ids"].shape[0]
    z = nc.dram_tensor("z_scratch", (NF * (WRAP + 1) + 1, S, TPC * Q), _mybir.dt.float32, kind="Internal").ap()
    out = nc.dram_tensor("out_y", (B,), _mybir.dt.float32, kind="ExternalOutput").ap()
    dlrm_tower(nc, args["r_dense_features"], args["ids"], [args[t] for t in _TABLES], args["w1_pairs"],
               args["w1_dense"], args["b_top1"], args["W_top2"], args["b_top2"], args["W_top3"], z, out)
    r = _run(nc, [arrays], core_ids=[0])
    y = r.results[0]["out_y"].reshape(B // P // TPC, S, TPC, Q)
    return _np.ascontiguousarray(y.transpose(3, 1, 0, 2)).reshape(B, 1)
```

```python
from contextlib import ExitStack

import concourse.bass as bass
from concourse import mybir

F32 = mybir.dt.float32
F32R = mybir.dt.float32r
U32 = mybir.dt.uint32
I32 = mybir.dt.int32
ACT = mybir.ActivationFunctionType
ALU = mybir.AluOpType

P = 128
NT = 26
NF = NT + 1
OH = 8
NX = NF - OH
SLOT = 32
S = P // SLOT
Q = P // S
TPP = 2
CW = TPP * P
STEPS = 8
GQ = TPP * Q // STEPS
TG = 4
NTG = -(-NX // TG)
NK = (NF - 1) // 2
WRAP = NF + NK
NOWRAP = NF - NK
KT = 3
FPK = NF // KT
KP = FPK * NK
assert OH == STEPS

SCHEDULE = []
for _k in range(STEPS):
    _tl, _at = divmod(_k, STEPS // TPP)
    SCHEDULE.append(("pick", _k))
    if _at == STEPS // TPP - 1:
        SCHEDULE += [("turn", _tl, 1), ("turn", _tl, 2)]
    SCHEDULE.append(("dots", _k))
    if _at == STEPS // TPP - 2:
        SCHEDULE += [("turn", _tl, 0)]
    if _at == STEPS // TPP - 1:
        SCHEDULE += [("turn", _tl, j) for j in range(3, NTG)]
    if _k == STEPS // 2 - 1:
        SCHEDULE.append(("mlp",))
INFLOW = [w for w in SCHEDULE if w[0] in ("pick", "turn")]
TP = len(INFLOW)
LAST_TURN = [INFLOW.index(("turn", tl, NTG - 1)) for tl in range(TPP)]
assert TP % 2 == 0


def wait_above_zero(eng, sem, count):
    if not isinstance(count, int) or count > 0:
        eng.wait_ge(sem, count)


def dlrm_tower(nc, dense, dense_cols, ids, ids_rows, gathered, picked, w1_pairs, w1_dense, b1, w2, b2, w3, z_dram,
               out):
    B, D = dense.shape
    TILES = B // P
    NP = TILES // TPP
    N1 = w1_dense.shape[1]
    N2 = w2.shape[1]
    M1 = N1 // P
    M2 = N2 // P
    MLP = M1 + M2 + 1
    V = picked[0].shape[0]
    VC = 8
    VP = V // VC
    HALF = VC // 2
    RAW = 3
    assert D == P and V == VP * VC and VP <= P and NF * NK == NF * (NF - 1) // 2

    with ExitStack() as ctx:
        def sb(name, shape, dt=F32):
            return ctx.enter_context(nc.sbuf_tensor(name, shape, dt))

        def psum(name, shape):
            return ctx.enter_context(nc.psum_tensor(name, shape, F32))

        def sem(name):
            return ctx.enter_context(nc.semaphore(name))

        ident = sb("ident", [P, P])
        idx = sb("idx", [P, TPP, NT], U32)
        x = sb("x", [P, TPP, NX, D])
        table_hl = sb("table_hl", [P, OH, VC, 2, D], F32R)
        row_id = sb("row_id", [P, VC])
        ids_b = sb("ids_b", [P, OH, CW], I32)
        onehot = sb("onehot", [P, VC, CW], F32R)
        xt = sb("xt", [P, 2, CW, SLOT])
        zs = sb("zs", [P, 2, NF, TPP, Q])
        zt = sb("zt", [P, KT + 1, CW])
        w1_sb = sb("w1_sb", [P, KT + 1, N1])
        w2_sb = sb("w2_sb", [P, M1, N2])
        w3_sb = sb("w3_sb", [P, M2])
        b1_sb = sb("b1_sb", [P, M1])
        b2_sb = sb("b2_sb", [P, M2])
        h1 = sb("h1", [P, M1, CW])
        h2 = sb("h2", [P, M2, CW])
        y_sb = sb("y_sb", [1, 2, CW])
        raw = zs[:].rearrange("p o g t q -> p (o g t q)")[0:VP, 0:RAW * VC * D].rearrange("p (r n) -> p r n", r=RAW)

        ps_t = psum("ps_t", [P, 2, TG * P])
        ps_g = psum("ps_g", [P, 2, GQ, P])
        ps_m = psum("ps_m", [P, 2, 2 * CW])

        ident_zeroed = sem("ident_zeroed")
        ident_ready = sem("ident_ready")
        pad_zeroed = sem("pad_zeroed")
        row_id_ready = sem("row_id_ready")
        raw_loaded = [sem(f"raw_loaded{i}") for i in range(RAW)]
        high_ready = sem("high_ready")
        low_ready = sem("low_ready")
        weights_loaded = sem("weights_loaded")
        ids_b_loaded = [sem(f"ids_b_loaded{i}") for i in range(2)]
        idx_loaded = [sem(f"idx_loaded{i}") for i in range(TPP)]
        dense_loaded = [sem(f"dense_loaded{i}") for i in range(TPP)]
        x_loaded = [sem(f"x_loaded{i}") for i in range(TPP)]
        onehot_made = sem("onehot_made")
        onehot_used = sem("onehot_used")
        tp_ready = sem("tp_ready")
        tp_moved = sem("tp_moved")
        dots_ready = sem("dots_ready")
        dots_moved = sem("dots_moved")
        z_stored = sem("z_stored")
        zt_loaded = sem("zt_loaded")
        mlp_ready = sem("mlp_ready")
        mlp_moved = sem("mlp_moved")
        y_stored = sem("y_stored")
        y_free = sem("y_free")

        Z_DMAS = 3 * S
        GATHERS = NX - 1

        block = ctx.enter_context(nc.Block())

        @block.sync
        def _(sp):
            def turn_pairs(u):
                src = zs[:, bass.ds(u % 2, 1)].rearrange("p o g t q -> p (o g) (t q)")
                for s in range(S):
                    at = SLOT * s
                    dst = z_dram[0:NF * WRAP, s].rearrange("(f g) q -> f g q", f=NF)
                    sp.dma_start(dst[0:NOWRAP, 1:NF], src[at:at + NOWRAP, 1:NF]).then_inc(z_stored, 16)
                    sp.dma_start(dst[NOWRAP:NF, NOWRAP + 1:NF], src[at + NOWRAP:at + NF, NOWRAP + 1:NF])\
                        .then_inc(z_stored, 16)
                    sp.dma_start(dst[NOWRAP:NF, NF:WRAP], src[at + NOWRAP:at + NF, 0:NK]).then_inc(z_stored, 16)

            def load_pairs(u):
                for k in range(KT):
                    row = FPK * k * (WRAP + 1) + 1
                    rows = z_dram[row:row + FPK * (WRAP + 1)].rearrange("(f g) s q -> f g (s q)", f=FPK)
                    sp.dma_start(zt[0:KP, k, :], rows[:, 0:NK]).then_inc(zt_loaded, 16)
                sp.dma_start(zt[:, KT, :], dense_cols[bass.ds(u, 1)].rearrange("o d n -> (o d) n"))\
                    .then_inc(zt_loaded, 16)

            def store_y(u):
                sp.wait_ge(mlp_moved, (u + 1) * MLP)
                sp.nop(nofuse=True)
                sp.dma_start(out[bass.ds(u * CW, CW)].rearrange("(o b) -> o b", o=1),
                             y_sb[:, bass.ds(u % 2, 1)].rearrange("p o n -> p (o n)")).then_inc(y_stored, 16)
                sp.wait_ge(y_stored, (u + 1) * 16)
                sp.nop(nofuse=True)
                sp.sem_inc(y_free, 1)

            def pair(u, first=False):
                sp.wait_ge(dots_moved, (u + 1) * STEPS)
                sp.nop(nofuse=True)
                turn_pairs(u)
                sp.wait_ge(z_stored, (u + 1) * (16 * Z_DMAS))
                sp.nop(nofuse=True)
                if not first:
                    sp.wait_ge(mlp_moved, (u - 1) * MLP + M1)
                    sp.nop(nofuse=True)
                load_pairs(u)
                sp.wait_ge(zt_loaded, (u + 1) * (16 * (KT + 1)))
                sp.nop(nofuse=True)
                if not first:
                    store_y(u - 1)

            sp.sem_inc(y_free, 2)
            for k in range(OH):
                if k >= RAW:
                    sp.wait_ge(low_ready, k - RAW + 1)
                sp.dma_start(raw[:, k % RAW], picked[k].rearrange("(p c) d -> p (c d)", c=VC))\
                    .then_inc(raw_loaded[k % RAW], 16)
            sp.dma_start(w1_sb[0:KP, 0:KT], w1_pairs.rearrange("(k p) n -> p k n", k=KT)).then_inc(weights_loaded, 16)
            sp.dma_start(w1_sb[:, KT], w1_dense).then_inc(weights_loaded, 16)
            sp.dma_start(w2_sb[:], w2.rearrange("(k p) n -> p k n", p=P)).then_inc(weights_loaded, 16)
            with nc.allow_non_contiguous_dma(reason="a few hundred words, once"):
                sp.dma_start(w3_sb[:], w3.rearrange("(k p) o -> p (k o)", p=P)).then_inc(weights_loaded, 16)
                sp.dma_start(b1_sb[:], b1.rearrange("(k p) -> p k", p=P)).then_inc(weights_loaded, 16)
                sp.dma_start(b2_sb[:], b2.rearrange("(k p) -> p k", p=P)).then_inc(weights_loaded, 16)
            pair(0, first=True)
            with sp.Fori(1, NP) as u:
                pair(u)
            store_y(NP - 1)

        @block.gpsimd
        def _(pool):
            def gather(tl):
                for f in range(GATHERS):
                    pool.indirect_dma_start(
                        x[:, tl, 1 + f, :], None, gathered[f][1],
                        bass.IndirectOffsetOnAxis(ap=idx[:, tl, gathered[f][0]:gathered[f][0] + 1], axis=0))\
                        .then_inc(x_loaded[tl], 16)

            nc.gpsimd.iota(row_id[:], pattern=[[1, VC]], base=0, channel_multiplier=VC,
                           allow_small_or_imprecise_dtypes=True).then_inc(row_id_ready, 1)
            nc.gpsimd.memset(ident[:], 0.0).then_inc(ident_zeroed, 1)
            nc.gpsimd.memset(xt[:, :, :, NF:SLOT], 0.0).then_inc(pad_zeroed, 1)
            pool.wait_ge(ident_zeroed, 1)
            nc.gpsimd.affine_select(out=ident[:], in_=ident[:], compare_op=ALU.not_equal, fill=1.0, base=0,
                                    pattern=[[-1, P]], channel_multiplier=1).then_inc(ident_ready, 1)
            for tl in range(TPP):
                pool.wait_ge(idx_loaded[tl], 16)
                gather(tl)
            with pool.Fori(1, NP) as u:
                for tl in range(TPP):
                    pool.wait_ge(idx_loaded[tl], (u + 1) * 16)
                    pool.nop(nofuse=True)
                    pool.wait_ge(tp_ready, (u - 1) * TP + (LAST_TURN[tl] + 1))
                    pool.nop(nofuse=True)
                    gather(tl)

        @block.tensor
        def _(pe):
            def pick(v, k, at):
                wait_above_zero(pe, tp_moved, v * TP + (at - 1))
                if isinstance(v, int) and v == 0:
                    pe.wait_ge(low_ready, k + 1)
                for c in range(VC):
                    if c % HALF == 0:
                        pe.wait_ge(onehot_made, v * (2 * OH) + (2 * k + c // HALF + 1))
                    for part in (1, 0):
                        mm = nc.tensor.matmul(ps_t[:, at % 2, 0:CW], table_hl[0:VP, k, c, part, :], onehot[0:VP, c, :],
                                              start=(c == 0 and part == 1), stop=(c == VC - 1 and part == 0))
                    if c == HALF - 1:
                        mm.then_inc(onehot_used, 1)
                mm.then_inc(tp_ready, 1)

            def turn(v, tl, j, at):
                if j == 0:
                    pe.wait_ge(dense_loaded[tl], (v + 1) * 16)
                    pe.wait_ge(x_loaded[tl], (v + 1) * (16 * GATHERS))
                wait_above_zero(pe, tp_moved, v * TP + (at - 1))
                fs = range(TG * j, min(TG * (j + 1), NX))
                for f in fs:
                    mm = nc.tensor.transpose(ps_t[:, at % 2, (f - fs[0]) * P:(f - fs[0] + 1) * P], x[:, tl, f, :],
                                             ident[:])
                mm.then_inc(tp_ready, 1)

            def dots(u, k, parity):
                if k == 0:
                    pe.wait_ge(tp_moved, (u + 1) * TP)
                wait_above_zero(pe, dots_moved, u * STEPS + (k - 1))
                for q in range(GQ):
                    a = (k * GQ + q) * S
                    mm = nc.tensor.matmul(ps_g[:, k % 2, q, 0:S * NF].rearrange("p (s f) -> p s f", s=S),
                                          xt[:, parity, a:a + S, :].rearrange("p s f -> p (s f)"),
                                          xt[:, parity, a:a + S, 0:NF], start=True, stop=True)
                mm.then_inc(dots_ready, 1)

            def mlp(u):
                pe.wait_ge(zt_loaded, (u + 1) * (16 * (KT + 1)))
                for m in range(M1):
                    wait_above_zero(pe, mlp_moved, u * MLP + max(m - 1, 0))
                    for k in range(KT + 1):
                        n = KP if k < KT else D
                        mm = nc.tensor.matmul(ps_m[:, m % 2, 0:CW], w1_sb[0:n, k, m * P:(m + 1) * P], zt[0:n, k, :],
                                              start=(k == 0), stop=(k == KT))
                    mm.then_inc(mlp_ready, 1)
                pe.wait_ge(mlp_moved, u * MLP + M1)
                for m in range(M2):
                    for k in range(M1):
                        mm = nc.tensor.matmul(ps_m[:, m % 2, 0:CW], w2_sb[:, k, m * P:(m + 1) * P], h1[:, k, :],
                                              start=(k == 0), stop=(k == M1 - 1))
                    mm.then_inc(mlp_ready, 1)
                pe.wait_ge(mlp_moved, u * MLP + (M1 + M2))
                for k in range(M2):
                    mm = nc.tensor.matmul(ps_m[0:1, 0, 0:CW], w3_sb[:, k:k + 1], h2[:, k, :],
                                          start=(k == 0), stop=(k == M2 - 1))
                mm.then_inc(mlp_ready, 1)

            def pair(u, parity, inflow=True, products=True, perceptron=True):
                at = 0
                for work in SCHEDULE:
                    if work[0] == "pick" and inflow:
                        pick(u + 1, work[1], at)
                        at += 1
                    elif work[0] == "turn" and inflow:
                        turn(u + 1, work[1], work[2], at)
                        at += 1
                    elif work[0] == "dots" and products:
                        dots(u, work[1], parity)
                    elif work[0] == "mlp" and perceptron:
                        mlp(u - 1)

            pe.wait_ge(ident_ready, 1)
            pe.wait_ge(pad_zeroed, 1)
            pair(-1, 1, products=False, perceptron=False)
            pe.wait_ge(weights_loaded, 16 * 6)
            pair(0, 0, perceptron=False)
            pair(1, 1)
            with pe.Fori(1, NP // 2 - 1) as i:
                pair(2 * i, 0)
                pair(2 * i + 1, 1)
            pair(NP - 2, 0)
            pair(NP - 1, 1, inflow=False, perceptron=False)
            mlp(NP - 2)
            mlp(NP - 1)

        @block.scalar
        def _(act):
            def load_tile(v, tl):
                t = v * TPP + tl
                act.dma_start(idx[:, tl, :],
                              ids.bitcast(U32).rearrange("(p t) f -> p t f", p=P)[:, bass.ds(t, 1)]
                              .rearrange("p o f -> p (o f)")).then_inc(idx_loaded[tl], 16)
                act.dma_start(x[:, tl, 0, :],
                              dense.rearrange("(p t) d -> p t d", p=P)[:, bass.ds(t, 1)]
                              .rearrange("p o d -> p (o d)")).then_inc(dense_loaded[tl], 16)

            def load_ids_b(v, h):
                ks = slice(h * OH // 2, (h + 1) * OH // 2)
                act.dma_start(ids_b[:, ks, :].rearrange("p k n -> p (k n)"),
                              ids_rows[bass.ds(v, 1), ks].rearrange("o k n -> o (k n)")
                              .to_broadcast([P, OH // 2 * CW])).then_inc(ids_b_loaded[h], 16)

            def move_features(v, work, at, parity, more):
                act.wait_ge(tp_ready, v * TP + (at + 1))
                if work[0] == "pick":
                    nc.scalar.copy(xt[:, parity, :, NX + work[1]], ps_t[:, at % 2, 0:CW]).then_inc(tp_moved, 1)
                    return
                tl, j = work[1:]
                n = min(TG, NX - TG * j)
                nc.scalar.copy(xt[:, parity, tl * P:(tl + 1) * P, TG * j:TG * j + n],
                               ps_t[:, at % 2, 0:n * P].rearrange("p (f b) -> p b f", f=n)).then_inc(tp_moved, 1)
                if j == NTG - 1 and more:
                    load_tile(v + 1, tl)

            def move_mlp(u, u_parity):
                for m in range(M1):
                    act.wait_ge(mlp_ready, u * MLP + (m + 1))
                    nc.scalar.activation(h1[:, m, :], ps_m[:, m % 2, 0:CW], ACT.Relu,
                                         bias=b1_sb[:, m:m + 1]).then_inc(mlp_moved, 1)
                for m in range(M2):
                    act.wait_ge(mlp_ready, u * MLP + (M1 + m + 1))
                    nc.scalar.activation(h2[:, m, :], ps_m[:, m % 2, 0:CW], ACT.Relu,
                                         bias=b2_sb[:, m:m + 1]).then_inc(mlp_moved, 1)
                act.wait_ge(mlp_ready, (u + 1) * MLP)
                act.wait_ge(y_free, u + 1)
                nc.scalar.copy(y_sb[:, u_parity, :], ps_m[0:1, 0, 0:CW]).then_inc(mlp_moved, 1)

            def pair(u, parity, perceptron=True, more=True):
                at = 0
                for work in SCHEDULE:
                    if work[0] in ("pick", "turn"):
                        if at == 0 and not (isinstance(u, int) and u < 1):
                            act.wait_ge(dots_moved, u * STEPS)
                        move_features(u + 1, work, at, parity, more)
                        at += 1
                    elif work[0] == "mlp" and perceptron:
                        move_mlp(u - 1, parity)
                    if work in (("pick", OH // 2 - 1), ("pick", OH - 1)) and more:
                        load_ids_b(u + 2, work[1] // (OH // 2))

            for tl in range(TPP):
                load_tile(0, tl)
            for h in range(2):
                load_ids_b(0, h)
            for k in range(OH):
                act.wait_ge(raw_loaded[k % RAW], 16 * (k // RAW + 1))
                nc.scalar.copy(table_hl[0:VP, k, :, 0, :], raw[:, k % RAW].rearrange("p (c d) -> p c d", c=VC))\
                    .then_inc(high_ready, 1)
            pair(-1, 0, perceptron=False)
            act.wait_ge(weights_loaded, 16 * 6)
            pair(0, 1, perceptron=False)
            pair(1, 0)
            with act.Fori(1, NP // 2 - 1) as i:
                pair(2 * i, 1)
                pair(2 * i + 1, 0)
            pair(NP - 2, 1, more=False)
            move_mlp(NP - 2, 0)
            move_mlp(NP - 1, 1)

        @block.vector
        def _(dve):
            def make_onehot(v, k):
                for c in range(VC):
                    if c == 0:
                        wait_above_zero(dve, onehot_used, v * OH + k)
                    elif c == HALF:
                        last_pick = INFLOW.index(("pick", (k - 1) % OH)) + 1
                        wait_above_zero(dve, tp_ready, v * TP + (last_pick if k > 0 else last_pick - TP))
                    last = nc.vector.tensor_scalar(onehot[0:VP, c, :], ids_b[0:VP, k, :],
                                                   row_id[0:VP, c:c + 1], None, ALU.is_equal)
                    if c % HALF == HALF - 1:
                        last.then_inc(onehot_made, 1)

            def move_dots(u, k, parity):
                dve.wait_ge(dots_ready, u * STEPS + (k + 1))
                if k == 0:
                    wait_above_zero(dve, z_stored, (u - 1) * (16 * Z_DMAS))
                tl, g = divmod(k, STEPS // TPP)
                for s in range(S):
                    rows = slice(SLOT * s, SLOT * s + NF)
                    last = nc.vector.tensor_copy(zs[rows, parity, :, tl, g * GQ:(g + 1) * GQ],
                                                 ps_g[rows, k % 2, :, s * NF:(s + 1) * NF]
                                                 .rearrange("p q g -> p g q"))
                last.then_inc(dots_moved, 1)

            def pair(u, parity, inflow=True, products=True):
                for k in range(STEPS + 1):
                    if k % (OH // 2) == 0 and k < STEPS and inflow:
                        dve.wait_ge(ids_b_loaded[k // (OH // 2)], (u + 2) * 16)
                    if k < STEPS and inflow:
                        make_onehot(u + 1, k)
                    if k >= 1 and products:
                        move_dots(u, k - 1, parity)

            dve.wait_ge(row_id_ready, 1)
            for k in range(OH):
                dve.wait_ge(high_ready, k + 1)
                nc.vector.tensor_tensor(out=table_hl[0:VP, k, :, 1, :],
                                        in0=raw[:, k % RAW].rearrange("p (c d) -> p c d", c=VC),
                                        in1=table_hl[0:VP, k, :, 0, :].bitcast(F32),
                                        op=ALU.subtract).then_inc(low_ready, 1)
            dve.wait_ge(low_ready, OH)
            pair(-1, 1, products=False)
            pair(0, 0)
            pair(1, 1)
            with dve.Fori(1, NP // 2 - 1) as i:
                pair(2 * i, 0)
                pair(2 * i + 1, 1)
            pair(NP - 2, 0)
            pair(NP - 1, 1, inflow=False)


def kernel(**inputs):
    import numpy as _np
    import concourse.bacc as _bacc
    from concourse import mybir as _mybir
    from concourse.bass_utils import run_bass_kernel_spmd as _run

    nc = _bacc.Bacc("TRN2", target_bir_lowering=False, num_devices=1)
    ids = _np.asarray(inputs["ids"])
    dense = _np.asarray(inputs["r_dense_features"])
    w1 = _np.asarray(inputs["W_top1"])
    B = ids.shape[0]
    tiles = B // P
    pairs = tiles // TPP

    rows = [inputs[f"tbl_{f}"].shape[0] for f in range(NT)]
    smallest = [f for f in range(NT) if rows[f] == min(rows)]
    picked = smallest[-OH:]
    gathered = [f for f in range(NT) if f not in picked]

    feature = [0] + [1 + t for t in gathered + picked]
    row = {}
    for i in range(NF):
        for j in range(i + 1, NF):
            row[i, j] = row[j, i] = len(row) // 2
    order = _np.array([row[feature[f], feature[(f + k) % NF]] for f in range(NF) for k in range(1, NK + 1)])

    given = {f"tbl_{f}": _np.asarray(inputs[f"tbl_{f}"]) for f in range(NT)}
    given.update({name: _np.asarray(inputs[name]) for name in ["b_top1", "W_top2", "b_top2", "W_top3"]})
    given["dense"] = dense
    given["ids"] = ids
    given["w1_pairs"] = w1[order]
    given["w1_dense"] = w1[len(row) // 2:]
    given["dense_cols"] = dense.reshape(Q, S, pairs, TPP, -1).transpose(2, 4, 1, 3, 0).reshape(pairs, -1, CW)
    given["ids_rows"] = ids[:, picked].reshape(P, pairs, TPP, OH).transpose(1, 3, 2, 0).reshape(pairs, OH, CW)
    arrays, a = {}, {}
    for name, value in given.items():
        value = _np.ascontiguousarray(value)
        arrays[f"in_{name}"] = value
        a[name] = nc.dram_tensor(f"in_{name}", value.shape, _mybir.dt.from_np(value.dtype), kind="ExternalInput").ap()
    z = nc.dram_tensor("z_scratch", (NF * (WRAP + 1) + 1, S, TPP * Q), _mybir.dt.float32, kind="Internal").ap()
    out = nc.dram_tensor("out_y", (B,), _mybir.dt.float32, kind="ExternalOutput").ap()
    dlrm_tower(nc, a["dense"], a["dense_cols"], a["ids"], a["ids_rows"], [(t, a[f"tbl_{t}"]) for t in gathered],
               [a[f"tbl_{t}"] for t in picked], a["w1_pairs"], a["w1_dense"], a["b_top1"], a["W_top2"],
               a["b_top2"], a["W_top3"], z, out)
    r = _run(nc, [arrays], core_ids=[0])
    y = r.results[0]["out_y"].reshape(pairs, S, TPP, Q)
    return _np.ascontiguousarray(y.transpose(3, 1, 0, 2)).reshape(B, 1)
```

```python
from contextlib import ExitStack

import concourse.bass as bass
from concourse import mybir

F32 = mybir.dt.float32
F32R = mybir.dt.float32r
U32 = mybir.dt.uint32
I32 = mybir.dt.int32
ACT = mybir.ActivationFunctionType
ALU = mybir.AluOpType

P = 128
NT = 26
NF = NT + 1
OH = 7
NX = NF - OH
S = 4
Q = P // S
TPP = 2
CW = TPP * P
STEPS = 8
GQ = TPP * Q // STEPS
TG = 4
NTG = -(-NX // TG)
NK = (NF - 1) // 2
ROW = NF - 1
KT = 3
FPK = NF // KT
KP = FPK * NK
PLANES = 2
PIECES = [(0, 0, NF), (1, 0, 2 * NF), (2, 32, 64), (2, 64, 3 * NF), (3, 64, 4 * NF)]
assert all(first >= NF * (s - 1) or s < PLANES for s, first, _ in PIECES)
assert all(first <= NF * s or (s, 32, first) in PIECES for s, first, _ in PIECES)
OH_HALVES = [(0, -(-OH // 2)), (-(-OH // 2), OH)]
assert OH <= STEPS

SCHEDULE = []
for _k in range(STEPS):
    _tl, _part = divmod(_k, STEPS // TPP)
    _turns = [("turn", _tl, j) for j in range(NTG)] if _part == STEPS // TPP - 1 else []
    if _k < OH:
        SCHEDULE.append(("pick", _k))
    if _k == STEPS // TPP + 2:
        SCHEDULE.append(("mlp2",))
    SCHEDULE += _turns[:2] + [("dots", _k)] + _turns[2:]
    if _k == STEPS // TPP + 1:
        SCHEDULE.append(("mlp1",))
SCHEDULE.insert(len(SCHEDULE) - 1, ("mlp3",))
SCHEDULE_0 = [w for w in SCHEDULE if w[0][:3] != "mlp"]
H = STEPS // TPP
DOTS = [("dots", k) for k in range(STEPS)]
PICKS = [("pick", k) for k in range(OH)]
LAST_TURNS = [("turn", TPP - 1, j) for j in range(NTG)]
FIRST_TILE = SCHEDULE[:SCHEDULE.index(("dots", H))]
REST = [w for two in zip(DOTS[H:], PICKS[H + 1:]) for w in two] + DOTS[OH - 1:] + [("mlp1",)]
INFLOW = [w for w in SCHEDULE if w[0] in ("pick", "turn")]
TP = len(INFLOW)
EXTRA_OF = [2, 3]
EARLY = len(EXTRA_OF)
EXTRA = max(EXTRA_OF)


def extras(v):
    return EXTRA_OF[v] if isinstance(v, int) and v < EARLY else 0


def extras_before(v):
    return sum(EXTRA_OF[:v] if isinstance(v, int) else EXTRA_OF)


def with_extra(works, v):
    at = works.index(("pick", OH - 1)) + 1
    return works[:at] + [("pick", OH + k) for k in range(extras(v))] + works[at:]


def inflow(v):
    return with_extra(INFLOW, v)


def groups_before(v):
    return v * TP + extras_before(v)


def feature_bank(v, parity, at):
    return (parity * TP + extras_before(v) + at) % 2


def picks_before(v):
    return v * OH + extras_before(v)


def wait_above_zero(eng, sem, count):
    if not isinstance(count, int) or count > 0:
        eng.wait_ge(sem, count)


def dlrm_tower(nc, dense, dense_cols, ids, ids_rows, ids_rows_extra, gathered, picked, w1_pairs, w1_dense, b1, w2,
               b2, w3, z_dram, out):
    B, D = dense.shape
    TILES = B // P
    NP = TILES // TPP
    N1 = w1_dense.shape[1]
    N2 = w2.shape[1]
    M1 = N1 // P
    M2 = N2 // P
    MLP = M1 + M2 + 1
    V = picked[0].shape[0]
    VC = 8
    VP = V // VC
    HALF = VC // 2
    assert D == P and V == VP * VC and VP <= P and NF * NK == NF * (NF - 1) // 2

    with ExitStack() as ctx:
        def sb(name, shape, dt=F32):
            return ctx.enter_context(nc.sbuf_tensor(name, shape, dt))

        def psum(name, shape):
            return ctx.enter_context(nc.psum_tensor(name, shape, F32))

        def sem(name):
            return ctx.enter_context(nc.semaphore(name))

        ident = sb("ident", [P, P])
        idx = sb("idx", [P, TPP, NT], U32)
        x = sb("x", [P, TPP, NX, D])
        table_hl = sb("table_hl", [P, OH, VC, 2, D], F32R)
        row_id = sb("row_id", [P, VC])
        ids_b = sb("ids_b", [P, OH, CW], I32)
        onehot = sb("onehot", [P, VC, CW], F32R)
        xt = sb("xt", [P, 2, CW, NF])
        zs = sb("zs", [P, 2, PLANES, NF, TPP, Q])
        zt = sb("zt", [P, KT + 1, CW])
        zt_hl = sb("zt_hl", [P, 2, KT + 1, CW], F32R)
        w1_hl = sb("w1_hl", [P, 2, KT + 1, N1], F32R)
        w2_sb = sb("w2_sb", [P, M1, N2])
        w3_sb = sb("w3_sb", [P, M2])
        b1_sb = sb("b1_sb", [P, M1])
        b2_sb = sb("b2_sb", [P, M2])
        h1 = sb("h1", [P, M1, CW])
        h2 = sb("h2", [P, M2, CW])
        h2w = sb("h2w", [P, CW])
        ones = sb("ones", [P, 1])
        y_sb = sb("y_sb", [1, 2, CW])
        TD = VC * D
        zs_room = [zs[:, i].rearrange("p r g t q -> p (r g t q)") for i in range(2)]
        w1_raw = zs_room[1][:, 0:(KT + 1) * N1].rearrange("p (k n) -> p k n", k=KT + 1)
        xt_room = xt[0:VP, 1].rearrange("p b f -> p (b f)")
        IN_XT = CW * NF // TD
        assert OH == IN_XT + 1 and (KT + 1) * N1 == 2 * TD and EARLY == 2
        assert 2 * TD + EXTRA * CW <= PLANES * NF * TPP * Q
        ids_extra = [room[:, 2 * TD:2 * TD + EXTRA * CW].bitcast(I32) for room in zs_room]
        assert EXTRA == 3 and (KT + 1) * CW == TD and M1 * CW == TD and (KT + 1) * N1 == 2 * TD
        raws = [xt_room[:, k * TD:(k + 1) * TD] for k in range(IN_XT)]
        raws += [zs_room[0][0:VP, 0:TD]]
        raws += [zt[0:VP].rearrange("p k n -> p (k n)"), h1[0:VP].rearrange("p k n -> p (k n)"),
                 zs_room[0][0:VP, TD:2 * TD]]
        tables = [table_hl[0:VP, k] for k in range(OH)]
        tables += [room.rearrange("p (c h d) -> p c h d", c=VC, h=2)
                   for room in (zt_hl[0:VP].rearrange("p h k n -> p (h k n)"),
                                w1_hl[0:VP, 0].rearrange("p k n -> p (k n)"),
                                w1_hl[0:VP, 1].rearrange("p k n -> p (k n)"))]

        ps_t = psum("ps_t", [P, 2, TG * P])
        ps_g = psum("ps_g", [P, 2, GQ, P])
        ps_m = psum("ps_m", [P, 2, 2 * CW])

        ident_zeroed = sem("ident_zeroed")
        ident_ready = sem("ident_ready")
        ones_ready = sem("ones_ready")
        row_id_ready = sem("row_id_ready")
        raw_loaded = [sem(f"raw_loaded{i}") for i in range(OH + EXTRA)]
        high_ready = sem("high_ready")
        low_ready = sem("low_ready")
        w1_loaded = sem("w1_loaded")
        w1_high_ready = sem("w1_high_ready")
        w1_ready = sem("w1_ready")
        weights_loaded = sem("weights_loaded")
        ids_extra_loaded = sem("ids_extra_loaded")
        ids_b_loaded = [sem(f"ids_b_loaded{i}") for i in range(2)]
        idx_loaded = [sem(f"idx_loaded{i}") for i in range(TPP)]
        dense_loaded = [sem(f"dense_loaded{i}") for i in range(TPP)]
        x_loaded = [sem(f"x_loaded{i}") for i in range(TPP)]
        onehot_made = sem("onehot_made")
        onehot_used = sem("onehot_used")
        tp_ready = sem("tp_ready")
        tp_moved = sem("tp_moved")
        dots_ready = sem("dots_ready")
        dots_moved = [sem(f"dots_moved{i}") for i in range(2)]
        z_stored = sem("z_stored")
        zt_loaded = sem("zt_loaded")
        zt_high_ready = sem("zt_high_ready")
        zt_ready = sem("zt_ready")
        mlp_ready = sem("mlp_ready")
        mlp_moved = sem("mlp_moved")
        h2w_begun = sem("h2w_begun")
        h2w_ready = sem("h2w_ready")
        y_stored = sem("y_stored")
        y_free = sem("y_free")

        Z_DMAS = S + PLANES

        def mlp_place(u, layer):
            if layer == 1:
                return -1 if isinstance(u, int) and u >= NP - 2 else 0
            if layer == 2:
                return M1
            return MLP - 1 + M1 if isinstance(u, int) and NP - 3 <= u < NP - 1 else M1 + M2

        def mlp_before(u, layer):
            return u * MLP + mlp_place(u, layer)

        def mlp_bank(u, parity, layer, m):
            return ps_m[:, (parity * MLP + mlp_place(u, layer) + m) % 2, 0:CW]
        GATHERS = NX - 1

        block = ctx.enter_context(nc.Block())

        @block.sync
        def _(sp):
            def turn_pairs(u):
                half = zs[:, bass.ds(u % 2, 1)].rearrange("p o r g t q -> p (o r) g (t q)")
                for s in range(S):
                    at = NF * s
                    src = half[:, s % PLANES]
                    sp.dma_start(z_dram[0:NF * ROW, s].rearrange("(f g) q -> f g q", f=NF),
                                 src[at:at + NF, 0:ROW]).then_inc(z_stored, 16)
                for plane in range(PLANES):
                    last = z_dram[NF * ROW + 1:NF * ROW + 1 + NK].rearrange("g s q -> s g q")
                    sp.dma_start(last[plane::PLANES],
                                 half[NF * (plane + 1) - 1:NF * S:NF * PLANES, plane, NF - 1 - NK:NF - 1])\
                        .then_inc(z_stored, 16)

            def load_pairs(u):
                for k in range(KT):
                    first = FPK * k * (ROW + 1) + 1
                    rows = z_dram[first:first + FPK * (ROW + 1)].rearrange("(f g) s q -> f g (s q)", f=FPK)
                    sp.dma_start(zt[0:KP, k, :], rows[:, 0:NK]).then_inc(zt_loaded, 16)

            def store_y(u):
                sp.wait_ge(mlp_moved, mlp_before(u, 3) + 1)
                sp.nop(nofuse=True)
                sp.dma_start(out[bass.ds(u * CW, CW)].rearrange("(o b) -> o b", o=1),
                             y_sb[:, bass.ds(u % 2, 1)].rearrange("p o n -> p (o n)")).then_inc(y_stored, 16)
                sp.wait_ge(y_stored, (u + 1) * 16)
                sp.nop(nofuse=True)
                sp.sem_inc(y_free, 1)

            def pair(u, first=False):
                for moved in dots_moved:
                    sp.wait_ge(moved, (u + 1) * (STEPS // 2))
                    sp.nop(nofuse=True)
                turn_pairs(u)
                if not first:
                    sp.wait_ge(zt_ready, u)
                    sp.nop(nofuse=True)
                sp.dma_start(zt[:, KT, :], dense_cols[bass.ds(u, 1)].rearrange("o d n -> (o d) n"))\
                    .then_inc(zt_loaded, 16)
                sp.wait_ge(z_stored, (u + 1) * (16 * Z_DMAS))
                sp.nop(nofuse=True)
                load_pairs(u)
                sp.wait_ge(zt_loaded, (u + 1) * (16 * (KT + 1)))
                sp.nop(nofuse=True)

            sp.sem_inc(y_free, 2)
            for k in range(OH + EXTRA):
                if k == OH:
                    sp.wait_ge(x_loaded[0], 16 * (GATHERS - extras(0)))
                sp.dma_start(raws[k], picked[k].rearrange("(p c) d -> p (c d)", c=VC)).then_inc(raw_loaded[k], 16)
            sp.dma_start(w1_raw[0:KP, 0:KT], w1_pairs.rearrange("(k p) n -> p k n", k=KT)).then_inc(w1_loaded, 16)
            sp.dma_start(w1_raw[:, KT], w1_dense).then_inc(w1_loaded, 16)
            sp.dma_start(w2_sb[:], w2.rearrange("(k p) n -> p k n", p=P)).then_inc(weights_loaded, 16)
            with nc.allow_non_contiguous_dma(reason="a few hundred words, once"):
                sp.dma_start(w3_sb[:], w3.rearrange("(k p) o -> p (k o)", p=P)).then_inc(weights_loaded, 16)
                sp.dma_start(b1_sb[:], b1.rearrange("(k p) -> p k", p=P)).then_inc(weights_loaded, 16)
                sp.dma_start(b2_sb[:], b2.rearrange("(k p) -> p k", p=P)).then_inc(weights_loaded, 16)
            sp.wait_ge(low_ready, OH + EXTRA)
            pair(0, first=True)
            with sp.Fori(1, NP - 2) as u:
                pair(u)
                store_y(u - 1)
            for u in (NP - 2, NP - 1):
                pair(u)
            for u in range(NP - 3, NP):
                store_y(u)

        @block.gpsimd
        def _(pool):
            def gather(tl, count=GATHERS):
                for f in range(count):
                    pool.indirect_dma_start(
                        x[:, tl, 1 + f, :], None, gathered[f][1],
                        bass.IndirectOffsetOnAxis(ap=idx[:, tl, gathered[f][0]:gathered[f][0] + 1], axis=0))\
                        .then_inc(x_loaded[tl], 16)

            nc.gpsimd.iota(row_id[:], pattern=[[1, VC]], base=0, channel_multiplier=VC,
                           allow_small_or_imprecise_dtypes=True).then_inc(row_id_ready, 1)
            nc.gpsimd.memset(ident[:], 0.0).then_inc(ident_zeroed, 1)
            nc.gpsimd.memset(ones[:], 1.0).then_inc(ones_ready, 1)
            pool.wait_ge(ident_zeroed, 1)
            nc.gpsimd.affine_select(out=ident[:], in_=ident[:], compare_op=ALU.not_equal, fill=1.0, base=0,
                                    pattern=[[-1, P]], channel_multiplier=1).then_inc(ident_ready, 1)
            for tl in range(TPP):
                pool.wait_ge(idx_loaded[tl], 16)
                gather(tl, GATHERS - extras(0))
            for tl in range(TPP):
                pool.wait_ge(idx_loaded[tl], 2 * 16)
                pool.wait_ge(tp_ready, inflow(0).index(("turn", tl, NTG - 1)) + 1)
                gather(tl, GATHERS - extras(1))
            with pool.Fori(EARLY, NP) as u:
                for tl in range(TPP):
                    pool.wait_ge(idx_loaded[tl], (u + 1) * 16)
                    pool.nop(nofuse=True)
                    last_turn = INFLOW.index(("turn", tl, NTG - 1))
                    pool.wait_ge(tp_ready, (u - 1) * TP + (extras_before(EARLY) + last_turn + 1))
                    pool.nop(nofuse=True)
                    gather(tl)

        @block.tensor
        def _(pe):
            def pick(v, k, at, bank):
                wait_above_zero(pe, tp_moved, groups_before(v) + (at - 1))
                if isinstance(v, int) and v < EARLY:
                    pe.wait_ge(low_ready, k + 1)
                for c in range(VC):
                    if c % HALF == 0:
                        pe.wait_ge(onehot_made, 2 * picks_before(v) + (2 * k + c // HALF + 1))
                    for part in (1, 0):
                        mm = nc.tensor.matmul(ps_t[:, bank, 0:CW], tables[k][:, c, part, :], onehot[0:VP, c, :],
                                              start=(c == 0 and part == 1), stop=(c == VC - 1 and part == 0))
                    if c == HALF - 1:
                        mm.then_inc(onehot_used, 1)
                mm.then_inc(tp_ready, 1)

            def turn(v, tl, j, at, bank):
                if j == 0:
                    pe.wait_ge(dense_loaded[tl], (v + 1) * 16)
                    pe.wait_ge(x_loaded[tl], (v + 1) * (16 * GATHERS) - 16 * extras_before(v + 1))
                wait_above_zero(pe, tp_moved, groups_before(v) + (at - 1))
                fs = range(TG * j, min(TG * (j + 1), NX - extras(v)))
                for f in fs:
                    mm = nc.tensor.transpose(ps_t[:, bank, (f - fs[0]) * P:(f - fs[0] + 1) * P], x[:, tl, f, :],
                                             ident[:])
                mm.then_inc(tp_ready, 1)

            def dots(u, k, parity):
                if k == 0:
                    pe.wait_ge(tp_moved, groups_before(u) + inflow(u).index(("turn", 1, 0)))
                elif k == STEPS // TPP:
                    pe.wait_ge(tp_moved, groups_before(u + 1))
                wait_above_zero(pe, dots_moved[k % 2], u * (STEPS // 2) + k // 2)
                for q in range(GQ):
                    a = (k * GQ + q) * S
                    four = xt[:, parity, a:a + S, :].rearrange("p s f -> p (s f)")
                    mm = nc.tensor.matmul(ps_g[0:S * NF, k % 2, q, 0:S * NF], four, four, start=True, stop=True)
                mm.then_inc(dots_ready, 1)

            def mlp1(u, parity):
                pe.wait_ge(zt_ready, u + 1)
                if isinstance(u, int) and u == 0:
                    pe.wait_ge(w1_ready, 2)
                for m in range(M1):
                    wait_above_zero(pe, mlp_moved, mlp_before(u, 1) + (m - 1))
                    products = [(k, w, z) for k in range(KT + 1) for w, z in ((1, 0), (0, 1), (0, 0))]
                    for k, w, z in products:
                        n = KP if k < KT else D
                        mm = nc.tensor.matmul(mlp_bank(u, parity, 1, m), w1_hl[0:n, w, k, m * P:(m + 1) * P],
                                              zt_hl[0:n, z, k, :], start=((k, w, z) == products[0]),
                                              stop=((k, w, z) == products[-1]))
                    mm.then_inc(mlp_ready, 1)

            def mlp2(u, parity):
                for m in range(M2):
                    pe.wait_ge(mlp_moved, mlp_before(u, 2) + (m - 1))
                    for k in range(M1):
                        if m == 0 and k == M1 - 1:
                            pe.wait_ge(mlp_moved, mlp_before(u, 1) + M1)
                        mm = nc.tensor.matmul(mlp_bank(u, parity, 2, m), w2_sb[:, k, m * P:(m + 1) * P], h1[:, k, :],
                                              start=(k == 0), stop=(k == M1 - 1))
                    mm.then_inc(mlp_ready, 1)

            def mlp3(u, parity):
                pe.wait_ge(h2w_ready, u + 1)
                pe.wait_ge(mlp_moved, mlp_before(u, 3) - 1)
                mm = nc.tensor.matmul(mlp_bank(u, parity, 3, 0)[0:1], ones[:], h2w[:], start=True, stop=True)
                mm.then_inc(mlp_ready, 1)

            def run(works, u, parity):
                for work in works:
                    if work[0] in ("pick", "turn"):
                        at = inflow(u + 1).index(work)
                        (pick if work[0] == "pick" else turn)(u + 1, *work[1:], at, feature_bank(u + 1, 1 - parity, at))
                    elif work[0] == "dots":
                        dots(u, work[1], parity)
                    else:
                        mlp[work[0]](u - 1, 1 - parity)

            mlp = {"mlp1": mlp1, "mlp2": mlp2, "mlp3": mlp3}
            pe.wait_ge(ident_ready, 1)
            run(inflow(0), -1, 1)
            pe.wait_ge(ones_ready, 1)
            pe.wait_ge(weights_loaded, 16 * 4)
            run(with_extra(SCHEDULE_0, 1), 0, 0)
            run(SCHEDULE, 1, 1)
            with pe.Fori(1, NP // 2 - 1) as i:
                run(SCHEDULE, 2 * i, 0)
                run(SCHEDULE, 2 * i + 1, 1)
            run(FIRST_TILE + REST, NP - 2, 0)
            run(DOTS[:H - 1], NP - 1, 1)
            run(LAST_TURNS[:2], NP - 2, 0)
            run(DOTS[H - 1:H], NP - 1, 1)
            run(LAST_TURNS[2:], NP - 2, 0)
            run(DOTS[H:], NP - 1, 1)
            mlp2(NP - 3, 1)
            for u, parity in ((NP - 2, 0), (NP - 1, 1)):
                mlp1(u, parity)
                mlp3(u - 1, 1 - parity)
                mlp2(u, parity)
            mlp3(NP - 1, 1)

        @block.scalar
        def _(act):
            def load_idx(v, tl):
                t = v * TPP + tl
                act.dma_start(idx[:, tl, :],
                              ids.bitcast(U32).rearrange("(p t) f -> p t f", p=P)[:, bass.ds(t, 1)]
                              .rearrange("p o f -> p (o f)")).then_inc(idx_loaded[tl], 16)

            def load_dense(v, tl):
                t = v * TPP + tl
                act.dma_start(x[:, tl, 0, :],
                              dense.rearrange("(p t) d -> p t d", p=P)[:, bass.ds(t, 1)]
                              .rearrange("p o d -> p (o d)")).then_inc(dense_loaded[tl], 16)

            def load_ids_b(v, h):
                ks = slice(*OH_HALVES[h])
                act.dma_start(ids_b[:, ks, :].rearrange("p k n -> p (k n)"),
                              ids_rows[bass.ds(v, 1), ks].rearrange("o k n -> o (k n)")
                              .to_broadcast([P, (ks.stop - ks.start) * CW])).then_inc(ids_b_loaded[h], 16)

            def move_features(v, work, at, bank, parity, more):
                act.wait_ge(tp_ready, groups_before(v) + (at + 1))
                if work[0] == "pick":
                    k = work[1]
                    feature = NX + k if k < OH else NX - 1 - (k - OH)
                    nc.scalar.copy(xt[:, parity, :, feature], ps_t[:, bank, 0:CW]).then_inc(tp_moved, 1)
                    return
                tl, j = work[1:]
                n = min(TG, NX - extras(v) - TG * j)
                nc.scalar.copy(xt[:, parity, tl * P:(tl + 1) * P, TG * j:TG * j + n],
                               ps_t[:, bank, 0:n * P].rearrange("p (f b) -> p b f", f=n)).then_inc(tp_moved, 1)
                if j == NTG - 1 and more:
                    load_idx(v + 1, tl)
                    load_dense(v + 1, tl)

            def move_dots(u, k, parity):
                act.wait_ge(dots_ready, u * STEPS + (k + 1))
                if k == 0:
                    wait_above_zero(act, z_stored, (u - 1) * (16 * Z_DMAS))
                tl, g = divmod(k, STEPS // TPP)
                for s, first, end in PIECES:
                    rows = slice(first, end)
                    last = nc.scalar.copy(zs[rows, parity, s % PLANES, :, tl, g * GQ:(g + 1) * GQ],
                                          ps_g[rows, k % 2, :, s * NF:(s + 1) * NF].rearrange("p q g -> p g q"))
                last.then_inc(dots_moved[0], 1)

            def move_mlp1(u, parity):
                for m in range(M1):
                    act.wait_ge(mlp_ready, mlp_before(u, 1) + (m + 1))
                    nc.scalar.activation(h1[:, m, :], mlp_bank(u, parity, 1, m), ACT.Relu,
                                         bias=b1_sb[:, m:m + 1]).then_inc(mlp_moved, 1)

            def move_mlp2(u, parity):
                for m in range(M2):
                    act.wait_ge(mlp_ready, mlp_before(u, 2) + (m + 1))
                    nc.scalar.activation(h2[:, m, :], mlp_bank(u, parity, 2, m), ACT.Relu,
                                         bias=b2_sb[:, m:m + 1]).then_inc(mlp_moved, 1)

            def move_mlp3(u, parity):
                act.wait_ge(mlp_ready, mlp_before(u, 3) + 1)
                act.wait_ge(y_free, u + 1)
                nc.scalar.copy(y_sb[:, parity, :], mlp_bank(u, parity, 3, 0)[0:1]).then_inc(mlp_moved, 1)

            def run(works, u, parity, more=True):
                for work in works:
                    if work[0] in ("pick", "turn"):
                        at = inflow(u + 1).index(work)
                        if at == 0 and not (isinstance(u, int) and u < 1):
                            for moved in dots_moved:
                                act.wait_ge(moved, u * (STEPS // 2))
                        move_features(u + 1, work, at, feature_bank(u + 1, 1 - parity, at), 1 - parity, more)
                        for h, (_, end) in enumerate(OH_HALVES):
                            if work == ("pick", end - 1) and more:
                                load_ids_b(u + 2, h)
                    elif work[0] == "dots":
                        if work[1] % 2 == 0:
                            move_dots(u, work[1], parity)
                    elif work[0] == "mlp1":
                        move_mlp1(u - 1, 1 - parity)
                    elif work[0] == "mlp2":
                        move_mlp2(u - 1, 1 - parity)
                    else:
                        move_mlp3(u - 1, 1 - parity)

            load_idx(0, 0)
            load_ids_b(0, 0)
            load_dense(0, 0)
            load_idx(0, 1)
            load_dense(0, 1)
            load_ids_b(0, 1)
            for v in range(EARLY):
                act.dma_start(ids_extra[v], ids_rows_extra[v:v + 1].rearrange("o k n -> o (k n)")
                              .to_broadcast([P, EXTRA * CW])).then_inc(ids_extra_loaded, 16)

            def round_tables(ks):
                for k in ks:
                    act.wait_ge(raw_loaded[k], 16)
                    nc.scalar.copy(tables[k][:, :, 0, :], raws[k].rearrange("p (c d) -> p c d", c=VC))\
                        .then_inc(high_ready, 1)

            works = inflow(0)
            round_tables(range(2))
            for k in range(H):
                round_tables([k + 2])
                run(works[k:k + 1], -1, 1)
            run(works[H:H + NTG], -1, 1)
            round_tables(range(H + 2, OH + EXTRA_OF[0]))
            run(works[H + NTG:-NTG], -1, 1)
            round_tables(range(OH + EXTRA_OF[0], OH + EXTRA))
            run(works[-NTG:], -1, 1)
            act.wait_ge(low_ready, OH + EXTRA)
            act.wait_ge(weights_loaded, 16 * 4)
            works = with_extra(SCHEDULE_0, 1)
            at = works.index(("pick", OH + extras(1) - 1)) + 1
            run(works[:at], 0, 0)
            act.wait_ge(w1_loaded, 32)
            nc.scalar.copy(w1_hl[0:KP, 0, 0:KT, :], w1_raw[0:KP, 0:KT, :]).then_inc(w1_high_ready, 1)
            nc.scalar.copy(w1_hl[:, 0, KT, :], w1_raw[:, KT, :]).then_inc(w1_high_ready, 1)
            run(works[at:], 0, 0)
            act.wait_ge(w1_ready, 2)
            run(SCHEDULE, 1, 1)
            with act.Fori(1, NP // 2 - 1) as i:
                run(SCHEDULE, 2 * i, 0)
                run(SCHEDULE, 2 * i + 1, 1)
            run(FIRST_TILE + REST, NP - 2, 0, more=False)
            run(DOTS[:H - 1], NP - 1, 1)
            run(LAST_TURNS[:2], NP - 2, 0, more=False)
            run(DOTS[H - 1:H], NP - 1, 1)
            run(LAST_TURNS[2:], NP - 2, 0, more=False)
            run(DOTS[H:], NP - 1, 1)
            move_mlp2(NP - 3, 1)
            for u, parity in ((NP - 2, 0), (NP - 1, 1)):
                move_mlp1(u, parity)
                move_mlp3(u - 1, 1 - parity)
                move_mlp2(u, parity)
            move_mlp3(NP - 1, 1)

        @block.vector
        def _(dve):
            def make_onehot(v, k):
                for h, (first, _) in enumerate(OH_HALVES):
                    if k == first:
                        dve.wait_ge(ids_b_loaded[h], (v + 1) * 16)
                if k == OH:
                    dve.wait_ge(ids_extra_loaded, 16 * EARLY)
                ids_k = ids_b[0:VP, k, :] if k < OH else ids_extra[v][0:VP, (k - OH) * CW:(k - OH + 1) * CW]
                for c in range(VC):
                    if c == 0:
                        wait_above_zero(dve, onehot_used, picks_before(v) + k)
                    elif c == HALF:
                        if k > 0:
                            wait_above_zero(dve, tp_ready, groups_before(v) + (inflow(v).index(("pick", k - 1)) + 1))
                        elif not (isinstance(v, int) and v == 0):
                            dve.wait_ge(tp_ready, groups_before(v) - NTG)
                    last = nc.vector.tensor_scalar(onehot[0:VP, c, :], ids_k,
                                                   row_id[0:VP, c:c + 1], None, ALU.is_equal)
                    if c % HALF == HALF - 1:
                        last.then_inc(onehot_made, 1)

            def move_dots(u, k, parity):
                dve.wait_ge(dots_ready, u * STEPS + (k + 1))
                if k == 1:
                    wait_above_zero(dve, z_stored, (u - 1) * (16 * Z_DMAS))
                tl, g = divmod(k, STEPS // TPP)
                for s, first, end in PIECES:
                    rows = slice(first, end)
                    last = nc.vector.tensor_copy(zs[rows, parity, s % PLANES, :, tl, g * GQ:(g + 1) * GQ],
                                                 ps_g[rows, k % 2, :, s * NF:(s + 1) * NF]
                                                 .rearrange("p q g -> p g q"))
                last.then_inc(dots_moved[1], 1)

            def split(k):
                dve.wait_ge(high_ready, k + 1)
                nc.vector.tensor_tensor(out=tables[k][:, :, 1, :],
                                        in0=raws[k].rearrange("p (c d) -> p c d", c=VC),
                                        in1=tables[k][:, :, 0, :].bitcast(F32),
                                        op=ALU.subtract).then_inc(low_ready, 1)

            def split_zt(u):
                dve.wait_ge(zt_loaded, (u + 1) * (16 * (KT + 1)))
                wait_above_zero(dve, mlp_ready, mlp_before(u - 1, 1) + M1)
                nc.vector.tensor_copy(zt_hl[0:KP, 0, 0:KT, :], zt[0:KP, 0:KT, :]).then_inc(zt_high_ready, 1)
                nc.vector.tensor_copy(zt_hl[:, 0, KT, :], zt[:, KT, :]).then_inc(zt_high_ready, 1)
                dve.wait_ge(zt_high_ready, (u + 1) * 2)
                nc.vector.tensor_tensor(out=zt_hl[0:KP, 1, 0:KT, :], in0=zt[0:KP, 0:KT, :],
                                        in1=zt_hl[0:KP, 0, 0:KT, :].bitcast(F32), op=ALU.subtract)
                nc.vector.tensor_tensor(out=zt_hl[:, 1, KT, :], in0=zt[:, KT, :],
                                        in1=zt_hl[:, 0, KT, :].bitcast(F32), op=ALU.subtract).then_inc(zt_ready, 1)

            def weigh_h2(u):
                dve.wait_ge(mlp_moved, mlp_before(u, 2) + 1)
                nc.vector.tensor_scalar(h2w[:], h2[:, 0, :], w3_sb[:, 0:1], None, ALU.mult).then_inc(h2w_begun, 1)
                dve.wait_ge(h2w_begun, u + 1)
                dve.wait_ge(mlp_moved, mlp_before(u, 2) + M2)
                nc.vector.scalar_tensor_tensor(out=h2w[:], in0=h2[:, 1, :], scalar=w3_sb[:, 1:2], in1=h2w[:],
                                               op0=ALU.mult, op1=ALU.add).then_inc(h2w_ready, 1)

            def pair(u, parity, perceptron=True, ks=range(STEPS)):
                for k in ks:
                    if k + 1 < OH + extras(u + 1):
                        make_onehot(u + 1, k + 1)
                    if k == OH - 1 and not extras(u + 1):
                        make_onehot(u + 2, 0)
                    if k == STEPS // TPP and perceptron:
                        split_zt(u - 1)
                    if k == STEPS - 1 and perceptron:
                        weigh_h2(u - 1)
                    if k % 2 == 1:
                        move_dots(u, k, parity)

            dve.wait_ge(row_id_ready, 1)
            make_onehot(0, 0)
            split(0)
            for k in range(1, OH + EXTRA):
                split(k)
                if k < OH + extras(0):
                    make_onehot(0, k)
            dve.wait_ge(low_ready, OH + EXTRA)
            dve.wait_ge(weights_loaded, 16 * 4)
            make_onehot(1, 0)
            pair(0, 0, perceptron=False, ks=range(STEPS - 1))
            for k in range(STEPS, OH + extras(1)):
                make_onehot(1, k)
            make_onehot(2, 0)
            dve.wait_ge(w1_high_ready, 1)
            nc.vector.tensor_tensor(out=w1_hl[0:KP, 1, 0:KT, :], in0=w1_raw[0:KP, 0:KT, :],
                                    in1=w1_hl[0:KP, 0, 0:KT, :].bitcast(F32), op=ALU.subtract).then_inc(w1_ready, 1)
            dve.wait_ge(w1_high_ready, 2)
            nc.vector.tensor_tensor(out=w1_hl[:, 1, KT, :], in0=w1_raw[:, KT, :],
                                    in1=w1_hl[:, 0, KT, :].bitcast(F32), op=ALU.subtract).then_inc(w1_ready, 1)
            move_dots(0, STEPS - 1, 0)
            dve.wait_ge(w1_ready, 2)
            pair(1, 1)
            with dve.Fori(1, NP // 2 - 1) as i:
                pair(2 * i, 0)
                pair(2 * i + 1, 1)
            pair(NP - 2, 0, ks=range(H))
            split_zt(NP - 3)
            make_onehot(NP - 1, H + 1)
            for k in range(H + 1, STEPS, 2):
                if k + 1 < OH:
                    make_onehot(NP - 1, k + 1)
                move_dots(NP - 2, k, 0)
            for k in range(1, STEPS, 2):
                move_dots(NP - 1, k, 1)
            split_zt(NP - 2)
            weigh_h2(NP - 3)
            split_zt(NP - 1)
            weigh_h2(NP - 2)
            weigh_h2(NP - 1)


def kernel(**inputs):
    import numpy as _np
    import concourse.bacc as _bacc
    from concourse import mybir as _mybir
    from concourse.bass_utils import run_bass_kernel_spmd as _run

    nc = _bacc.Bacc("TRN2", target_bir_lowering=False, num_devices=1, dynamic_dma_scratch_size=8192)
    ids = _np.asarray(inputs["ids"])
    dense = _np.asarray(inputs["r_dense_features"])
    w1 = _np.asarray(inputs["W_top1"])
    B = ids.shape[0]
    tiles = B // P
    pairs = tiles // TPP

    rows = [inputs[f"tbl_{f}"].shape[0] for f in range(NT)]
    smallest = [f for f in range(NT) if rows[f] == min(rows)]
    picked = smallest[-OH:]
    extra = smallest[-OH - EXTRA:-OH]
    gathered = [f for f in range(NT) if f not in picked + extra] + extra[::-1]

    feature = [0] + [1 + t for t in gathered + picked]
    row = {}
    for i in range(NF):
        for j in range(i + 1, NF):
            row[i, j] = row[j, i] = len(row) // 2
    pair_of = [(f, f + k) if f + k < ROW else (f + 1, f + k - ROW) for f in range(NF - 1) for k in range(1, NK + 1)]
    pair_of += [(NF - 1, k) for k in range(NF - 1 - NK, NF - 1)]
    order = _np.array([row[feature[f], feature[g]] for f, g in pair_of])

    given = {f"tbl_{f}": _np.asarray(inputs[f"tbl_{f}"]) for f in range(NT)}
    given.update({name: _np.asarray(inputs[name]) for name in ["b_top1", "W_top2", "b_top2", "W_top3"]})
    given["dense"] = dense
    given["ids"] = ids
    given["w1_pairs"] = w1[order]
    given["w1_dense"] = w1[len(row) // 2:]
    given["dense_cols"] = dense.reshape(Q, S, pairs, TPP, -1).transpose(2, 4, 1, 3, 0).reshape(pairs, -1, CW)
    given["ids_rows"] = ids[:, picked].reshape(P, pairs, TPP, OH).transpose(1, 3, 2, 0).reshape(pairs, OH, CW)
    given["ids_rows_extra"] = ids[:, extra].reshape(P, pairs, TPP, EXTRA).transpose(1, 3, 2, 0)[:EARLY]\
        .reshape(EARLY, EXTRA, CW)
    arrays, a = {}, {}
    for name, value in given.items():
        value = _np.ascontiguousarray(value)
        arrays[f"in_{name}"] = value
        a[name] = nc.dram_tensor(f"in_{name}", value.shape, _mybir.dt.from_np(value.dtype), kind="ExternalInput").ap()
    z = nc.dram_tensor("z_scratch", (NF * (ROW + 1) + 1, S, TPP * Q), _mybir.dt.float32, kind="Internal").ap()
    out = nc.dram_tensor("out_y", (B,), _mybir.dt.float32, kind="ExternalOutput").ap()
    dlrm_tower(nc, a["dense"], a["dense_cols"], a["ids"], a["ids_rows"], a["ids_rows_extra"],
               [(t, a[f"tbl_{t}"]) for t in gathered],
               [a[f"tbl_{t}"] for t in picked + extra], a["w1_pairs"], a["w1_dense"], a["b_top1"], a["W_top2"],
               a["b_top2"], a["W_top3"], z, out)
    r = _run(nc, [arrays], core_ids=[0])
    y = r.results[0]["out_y"].reshape(pairs, S, TPP, Q)
    return _np.ascontiguousarray(y.transpose(3, 1, 0, 2)).reshape(B, 1)
```
